# Optimizing a Trainium2 kernel written in Bass

```python
import numpy as np
import jax
import jax.numpy as jnp

def _softmax(x, axis=-1):
    return jax.nn.softmax(x, axis=axis)

def _gelu(x):
    return jax.nn.gelu(x, approximate=True)

def _silu(x):
    return jax.nn.silu(x)

def _sigmoid(x):
    return jax.nn.sigmoid(x)

def _layernorm(x, axis=-1, eps=1e-05):
    m = jnp.mean(x, axis=axis, keepdims=True)
    v = jnp.var(x, axis=axis, keepdims=True)
    return (x - m) / jnp.sqrt(v + eps)

def _scatter_add(tgt, idx, src, axis=0):
    return tgt.at[idx].add(src)

def _segment_sum(src, seg, n):
    return jax.ops.segment_sum(src, seg, n)
kernel_name = 'mk_dlrm_tower_d1_rec_r8_3512b1'

def setup_inputs(seed: int=0):
    np.random.seed(seed)
    _w = jnp.asarray

    def _rec_inputs():
        import jax
        import jax.numpy as jnp
        _tk = jax.random.key(seed)
        ids = jnp.stack([jax.random.randint(jax.random.fold_in(_tk, 200 + f), (512,), 0, v, jnp.int32) for f, v in enumerate([125000, 1250, 1000, 12500, 12500, 1250, 1000, 1000, 1000, 1250, 1000, 1000, 1250, 1250, 1000, 1250, 12500, 12500, 1000, 1000, 12500, 1250, 1250, 1000, 1250, 1000])], axis=1)
        tbl_0 = 0.05 * jax.random.normal(jax.random.fold_in(_tk, 500 + 0), (125000, 128), jnp.float32)
        tbl_1 = 0.05 * jax.random.normal(jax.random.fold_in(_tk, 500 + 1), (1250, 128), jnp.float32)
        tbl_2 = 0.05 * jax.random.normal(jax.random.fold_in(_tk, 500 + 2), (1000, 128), jnp.float32)
        tbl_3 = 0.05 * jax.random.normal(jax.random.fold_in(_tk, 500 + 3), (12500, 128), jnp.float32)
        tbl_4 = 0.05 * jax.random.normal(jax.random.fold_in(_tk, 500 + 4), (12500, 128), jnp.float32)
        tbl_5 = 0.05 * jax.random.normal(jax.random.fold_in(_tk, 500 + 5), (1250, 128), jnp.float32)
        tbl_6 = 0.05 * jax.random.normal(jax.random.fold_in(_tk, 500 + 6), (1000, 128), jnp.float32)
        tbl_7 = 0.05 * jax.random.normal(jax.random.fold_in(_tk, 500 + 7), (1000, 128), jnp.float32)
        tbl_8 = 0.05 * jax.random.normal(jax.random.fold_in(_tk, 500 + 8), (1000, 128), jnp.float32)
        tbl_9 = 0.05 * jax.random.normal(jax.random.fold_in(_tk, 500 + 9), (1250, 128), jnp.float32)
        tbl_10 = 0.05 * jax.random.normal(jax.random.fold_in(_tk, 500 + 10), (1000, 128), jnp.float32)
        tbl_11 = 0.05 * jax.random.normal(jax.random.fold_in(_tk, 500 + 11), (1000, 128), jnp.float32)
        tbl_12 = 0.05 * jax.random.normal(jax.random.fold_in(_tk, 500 + 12), (1250, 128), jnp.float32)
        tbl_13 = 0.05 * jax.random.normal(jax.random.fold_in(_tk, 500 + 13), (1250, 128), jnp.float32)
        tbl_14 = 0.05 * jax.random.normal(jax.random.fold_in(_tk, 500 + 14), (1000, 128), jnp.float32)
        tbl_15 = 0.05 * jax.random.normal(jax.random.fold_in(_tk, 500 + 15), (1250, 128), jnp.float32)
        tbl_16 = 0.05 * jax.random.normal(jax.random.fold_in(_tk, 500 + 16), (12500, 128), jnp.float32)
        tbl_17 = 0.05 * jax.random.normal(jax.random.fold_in(_tk, 500 + 17), (12500, 128), jnp.float32)
        tbl_18 = 0.05 * jax.random.normal(jax.random.fold_in(_tk, 500 + 18), (1000, 128), jnp.float32)
        tbl_19 = 0.05 * jax.random.normal(jax.random.fold_in(_tk, 500 + 19), (1000, 128), jnp.float32)
        tbl_20 = 0.05 * jax.random.normal(jax.random.fold_in(_tk, 500 + 20), (12500, 128), jnp.float32)
        tbl_21 = 0.05 * jax.random.normal(jax.random.fold_in(_tk, 500 + 21), (1250, 128), jnp.float32)
        tbl_22 = 0.05 * jax.random.normal(jax.random.fold_in(_tk, 500 + 22), (1250, 128), jnp.float32)
        tbl_23 = 0.05 * jax.random.normal(jax.random.fold_in(_tk, 500 + 23), (1000, 128), jnp.float32)
        tbl_24 = 0.05 * jax.random.normal(jax.random.fold_in(_tk, 500 + 24), (1250, 128), jnp.float32)
        tbl_25 = 0.05 * jax.random.normal(jax.random.fold_in(_tk, 500 + 25), (1000, 128), jnp.float32)
        _rk = jax.random.fold_in(_tk, 7)
        r_dense_features = -0.000292821 + 1.00034 * jax.random.normal(jax.random.fold_in(_rk, 101), (512, 128), jnp.float32)
        W_top1 = 0.0405887 * jax.random.normal(jax.random.fold_in(_tk, 801), (607, 512), jnp.float32)
        W_top2 = 0.0441942 * jax.random.normal(jax.random.fold_in(_tk, 802), (512, 256), jnp.float32)
        W_top3 = 0.0625 * jax.random.normal(jax.random.fold_in(_tk, 803), (256, 1), jnp.float32)
        b_top1 = jnp.zeros((512,), jnp.float32)
        b_top2 = jnp.zeros((256,), jnp.float32)
        return (r_dense_features, ids, tbl_0, tbl_1, tbl_2, tbl_3, tbl_4, tbl_5, tbl_6, tbl_7, tbl_8, tbl_9, tbl_10, tbl_11, tbl_12, tbl_13, tbl_14, tbl_15, tbl_16, tbl_17, tbl_18, tbl_19, tbl_20, tbl_21, tbl_22, tbl_23, tbl_24, tbl_25, W_top1, b_top1, W_top2, b_top2, W_top3)
    r_dense_features, ids, tbl_0, tbl_1, tbl_2, tbl_3, tbl_4, tbl_5, tbl_6, tbl_7, tbl_8, tbl_9, tbl_10, tbl_11, tbl_12, tbl_13, tbl_14, tbl_15, tbl_16, tbl_17, tbl_18, tbl_19, tbl_20, tbl_21, tbl_22, tbl_23, tbl_24, tbl_25, W_top1, b_top1, W_top2, b_top2, W_top3 = _rec_inputs()

    def _L0_rec_setup():
        import jax, jax.numpy as jnp
        import numpy as np
        F = 26
        _TRIU_I, _TRIU_J = np.triu_indices(F + 1, k=1)
        key = jax.random.key(seed)
        k1, k2 = jax.random.split(key)
        B, D = (4096, 128)
        dense_features = jax.random.normal(k1, (B, D), dtype=jnp.float32)
        sparse_features = jax.random.normal(k2, (B, F, D), dtype=jnp.float32)
        return {'dense_features': dense_features, 'sparse_features': sparse_features}
    _L0_rec_all = _L0_rec_setup()
    _L0_rec_in = {k: v for k, v in _L0_rec_all.items() if k in ()}
    del _L0_rec_all
    return {'r_dense_features': r_dense_features, 'ids': ids, 'tbl_0': tbl_0, 'tbl_1': tbl_1, 'tbl_2': tbl_2, 'tbl_3': tbl_3, 'tbl_4': tbl_4, 'tbl_5': tbl_5, 'tbl_6': tbl_6, 'tbl_7': tbl_7, 'tbl_8': tbl_8, 'tbl_9': tbl_9, 'tbl_10': tbl_10, 'tbl_11': tbl_11, 'tbl_12': tbl_12, 'tbl_13': tbl_13, 'tbl_14': tbl_14, 'tbl_15': tbl_15, 'tbl_16': tbl_16, 'tbl_17': tbl_17, 'tbl_18': tbl_18, 'tbl_19': tbl_19, 'tbl_20': tbl_20, 'tbl_21': tbl_21, 'tbl_22': tbl_22, 'tbl_23': tbl_23, 'tbl_24': tbl_24, 'tbl_25': tbl_25, 'W_top1': W_top1, 'b_top1': b_top1, 'W_top2': W_top2, 'b_top2': b_top2, 'W_top3': W_top3}

def reference(r_dense_features, ids, tbl_0, tbl_1, tbl_2, tbl_3, tbl_4, tbl_5, tbl_6, tbl_7, tbl_8, tbl_9, tbl_10, tbl_11, tbl_12, tbl_13, tbl_14, tbl_15, tbl_16, tbl_17, tbl_18, tbl_19, tbl_20, tbl_21, tbl_22, tbl_23, tbl_24, tbl_25, W_top1, b_top1, W_top2, b_top2, W_top3):
    import jax
    import jax.numpy as jnp

    def _L0_rec_ref(dense_features, sparse_features):
        import jax, jax.numpy as jnp
        import numpy as np
        F = 26
        _TRIU_I, _TRIU_J = np.triu_indices(F + 1, k=1)
        combined = jnp.concatenate([dense_features[:, None, :], sparse_features], axis=1)
        interactions = jnp.einsum('bfd,bgd->bfg', combined, combined)
        interactions_flat = interactions[:, _TRIU_I, _TRIU_J]
        return jnp.concatenate([dense_features, interactions_flat], axis=1)
    e = jnp.stack([tbl_0[ids[:, 0]], tbl_1[ids[:, 1]], tbl_2[ids[:, 2]], tbl_3[ids[:, 3]], tbl_4[ids[:, 4]], tbl_5[ids[:, 5]], tbl_6[ids[:, 6]], tbl_7[ids[:, 7]], tbl_8[ids[:, 8]], tbl_9[ids[:, 9]], tbl_10[ids[:, 10]], tbl_11[ids[:, 11]], tbl_12[ids[:, 12]], tbl_13[ids[:, 13]], tbl_14[ids[:, 14]], tbl_15[ids[:, 15]], tbl_16[ids[:, 16]], tbl_17[ids[:, 17]], tbl_18[ids[:, 18]], tbl_19[ids[:, 19]], tbl_20[ids[:, 20]], tbl_21[ids[:, 21]], tbl_22[ids[:, 22]], tbl_23[ids[:, 23]], tbl_24[ids[:, 24]], tbl_25[ids[:, 25]]], axis=1)
    z = _L0_rec_ref(r_dense_features, e)
    z = z.reshape(z.shape[0], -1)
    h = jnp.concatenate([z, r_dense_features], axis=1)
    h = jnp.maximum(h @ W_top1 + b_top1, 0.0)
    h = jnp.maximum(h @ W_top2 + b_top2, 0.0)
    y = h @ W_top3
    return y

_drawn_inputs = setup_inputs


def setup_inputs(seed=0):
    import zlib

    import numpy as np

    out = dict(_drawn_inputs(seed))
    spreads = {'b_top1': (0.0, 0.1), 'b_top2': (0.0, 0.1)}
    factors = {}
    for name, (base, spread) in spreads.items():
        noise = np.random.default_rng([zlib.crc32(name.encode()), seed]).standard_normal(out[name].shape)
        drawn = base * np.exp(spread * noise) if base else spread * noise
        out[name] = jnp.asarray(drawn.astype(out[name].dtype))
    for name, factor in factors.items():
        out[name] = (out[name] * factor).astype(out[name].dtype)
    return out
```

```python
from contextlib import ExitStack

import concourse.bass as bass
from concourse import mybir

F32 = mybir.dt.float32
F32R = mybir.dt.float32r
I32 = mybir.dt.int32
ALU = mybir.AluOpType
ACT = mybir.ActivationFunctionType

P = 128
D = 128
BATCH = 512
BLOCKS = BATCH // P
TABLES = 26
SLOTS = TABLES + 1
PAD = 32
Q = 4
CHUNKS = 7
GCOLS = Q * CHUNKS
HID1, HID2 = 512, 256
NC1 = HID1 // P

SELECTED = (2, 6, 7, 8, 10, 11)
GATHERED = tuple(t for t in range(TABLES) if t not in SELECTED)
SEL = len(SELECTED)
EARLY = SEL + 1
SEL_ROWS = 1024
KSEL = SEL_ROWS // P
NG = len(GATHERED)
GROUPS = [list(range(i, min(i + 4, NG))) for i in range(0, NG, 4)]
NGRP = len(GROUPS)
DVE_GRPS = (NGRP + 1) // 2
ACT_GRPS = NGRP // 2
TILES = 4
PER_TILE = P // Q // TILES


def build(nc, idx_d, sel_ids_d, row_id_d, ident_d, dense_t_d, sel_tbl_d, gather_tbls,
          w1_pairs_d, w1_dense_d, b1_d, w2_d, b2_d, w3_d, y_d):
    ctx = ExitStack()
    with ctx:
        def sb(name, shape, dt=F32):
            return ctx.enter_context(nc.sbuf_tensor(name, shape, dt))

        def ps(name, shape):
            return ctx.enter_context(nc.psum_tensor(name, shape, F32))

        def sem(name):
            return ctx.enter_context(nc.semaphore(name))

        idx = sb("idx", [P, BLOCKS, NG], I32)
        sel_ids = sb("sel_ids", [P, SEL, BATCH], I32)
        row_id = sb("row_id", [P, KSEL])
        ident = sb("ident", [P, P])
        sel_tbl = [sb(f"sel_tbl{i}", [P, KSEL, D]) for i in range(SEL)]
        tbl_hi = [sb(f"tbl_hi{i}", [P, KSEL, D], F32R) for i in range(2)]
        tbl_lo = [sb(f"tbl_lo{i}", [P, KSEL, D], F32R) for i in range(2)]
        onehot = [sb(f"onehot{i}", [P, KSEL, BATCH], F32R) for i in range(2)]
        early = sb("early", [P, EARLY, BATCH])
        rows = sb("rows", [P, NG, D])
        feat_t = sb("feat_t", [P, P, PAD])
        pairs = sb("pairs", [P, CHUNKS, P])
        w1_pairs = sb("w1_pairs", [P, CHUNKS, HID1])
        w1_dense2 = sb("w1_dense2", [P, 2, HID1])
        w1_dense = sb("w1_dense", [P, HID1])
        b1 = sb("b1", [P, NC1])
        w2 = sb("w2", [P, NC1, HID2])
        b2 = sb("b2", [1, HID2])
        ones = sb("ones", [1, P])
        w3 = sb("w3", [P, HID2])
        hid1_t = sb("hid1_t", [P, NC1, P])
        hid2 = sb("hid2", [P, HID2])
        y = sb("y", [P, BLOCKS])

        ps_tr = [ps(f"ps_tr{i}", [P, 4, P]) for i in range(2)]
        ps_gram = [ps(f"ps_gram{i}", [P, 2, 512]) for i in range(2)]
        ps_l1 = [ps(f"ps_l1{i}", [P, 2, 256]) for i in range(2)]
        ps_sel = [ps_gram[i // 2][:, i % 2, :] for i in range(4)]
        ps_l2 = ps_gram[0][:, 0, 0:HID2]

        idx_in = sem("idx_in")
        row_id_in = sem("row_id_in")
        sel_ids_in = [sem(f"sel_ids_in{i}") for i in range(2)]
        sel_tbl_in = [sem(f"sel_tbl_in{i}") for i in range(SEL)]
        ident_in = sem("ident_in")
        dense_in = sem("dense_in")
        w1_dense_in = sem("w1_dense_in")
        w1_in = sem("w1_in")
        w2_in = sem("w2_in")
        b1_in = sem("b1_in")
        w3_in = sem("w3_in")
        rows_in = [sem(f"rows_in{i}") for i in range(NGRP)]
        ones_set = sem("ones_set")
        w1_dense_sum = sem("w1_dense_sum")
        hi_done = sem("hi_done")
        lo_done = sem("lo_done")
        onehot_done = sem("onehot_done")
        sel_done = sem("sel_done")
        early_psum = sem("early_psum")
        early_feat = sem("early_feat")
        tr_done = sem("tr_done")
        feat_dve = sem("feat_dve")
        feat_act = sem("feat_act")
        gram_done = sem("gram_done")
        pairs_dve = sem("pairs_dve")
        pairs_act = sem("pairs_act")
        l1_done = sem("l1_done")
        hid1_act = sem("hid1_act")
        hid1_dve = sem("hid1_dve")
        l2_done = sem("l2_done")
        y_done = sem("y_done")
        out_done = sem("out_done")

        block = ctx.enter_context(nc.Block())

        def pairs_out(engine_copy, tile, quads):
            src = ps_gram[tile % 2][:, :, 0:PER_TILE // 2 * Q * GCOLS].rearrange(
                "p h (n j k q) -> p h n j k q", n=PER_TILE // 2, j=Q, k=CHUNKS)
            dst = pairs[:, :, tile * PER_TILE * Q:(tile + 1) * PER_TILE * Q].rearrange(
                "p k (h n j) -> p h n j k", h=2, j=Q)
            for j in quads:
                for q in range(Q):
                    last = engine_copy(dst[32 * q:32 * q + 32, :, :, j, :],
                                       src[32 * j:32 * j + 32, :, :, j, :, q])
            return last

        @block.sync
        def _(sp):
            sp.dma_start(sel_ids[:, 0, :], sel_ids_d[0, :].partition_broadcast(P)).then_inc(sel_ids_in[0], 16)
            sp.dma_start(row_id[:], row_id_d).then_inc(row_id_in, 16)
            sp.dma_start(sel_tbl[0][:], sel_tbl_d[0]).then_inc(sel_tbl_in[0], 16)
            sp.dma_start(sel_ids[:, 1:SEL, :].rearrange("p t b -> p (t b)"),
                         sel_ids_d[1:SEL, :].rearrange("t b -> (t b)").partition_broadcast(P)
                         ).then_inc(sel_ids_in[1], 16)
            for i in range(1, SEL):
                sp.dma_start(sel_tbl[i][:], sel_tbl_d[i]).then_inc(sel_tbl_in[i], 16)
            sp.dma_start(early[:, 0, :], dense_t_d).then_inc(dense_in, 16)
            sp.dma_start(ident[:], ident_d).then_inc(ident_in, 16)
            sp.dma_start(w1_dense2[:], w1_dense_d).then_inc(w1_dense_in, 16)
            sp.dma_start(w1_pairs[:], w1_pairs_d).then_inc(w1_in, 16)
            sp.dma_start(b1[:], b1_d).then_inc(b1_in, 16)
            sp.dma_start(w2[:], w2_d).then_inc(w2_in, 16)
            sp.dma_start(b2[:], b2_d).then_inc(w2_in, 16)
            sp.dma_start(w3[:], w3_d.partition_broadcast(P)).then_inc(w3_in, 16)
            sp.wait_ge(y_done, BLOCKS)
            sp.dma_start(y_d, y[:]).then_inc(out_done, 16)
            sp.wait_ge(out_done, 16)

        @block.gpsimd
        def _(pool):
            pool.dma_start(idx[:], idx_d).then_inc(idx_in, 16)
            pool.wait_ge(idx_in, 16)
            for c in range(BLOCKS):
                for i, group in enumerate(GROUPS):
                    if c >= 1:
                        pool.wait_ge(tr_done, (c - 1) * NGRP + i + 1)
                    for t in group:
                        pool.indirect_dma_start(
                            out=rows[:, t, :], out_offset=None, in_=gather_tbls[t],
                            in_offset=bass.IndirectOffsetOnAxis(ap=idx[:, c, t:t + 1], axis=0),
                        ).then_inc(rows_in[i], 16)

        @block.tensor
        def _(pe):
            def transposes(block_no, i):
                group = GROUPS[i]
                pe.wait_ge(rows_in[i], (block_no + 1) * (16 * len(group)))
                for n, t in enumerate(group):
                    last = nc.tensor.transpose(ps_tr[i % 2][:, n, :], rows[:, t, :], ident[:])
                last.then_inc(tr_done, 1)

            def gram_and_mlp(c):
                pe.wait_ge(feat_dve, c * DVE_GRPS + 1)
                pe.wait_ge(feat_act, c * ACT_GRPS + NGRP)
                pe.wait_ge(early_feat, c + 1)
                for tile in range(TILES):
                    if tile >= 2:
                        pe.wait_ge(pairs_dve, c * TILES + tile - 1)
                        pe.wait_ge(pairs_act, c * TILES + tile - 1)
                    for n in range(PER_TILE):
                        s = (tile * PER_TILE + n) * Q
                        half, m = divmod(n, PER_TILE // 2)
                        last = nc.tensor.matmul(
                            ps_gram[tile % 2][:, half, m * Q * GCOLS:(m + 1) * Q * GCOLS],
                            feat_t[:, s:s + Q, :].rearrange("d s f -> d (s f)"),
                            feat_t[:, s:s + Q, 0:GCOLS], start=True, stop=True)
                    last.then_inc(gram_done, 1)
                for h in range(NC1):
                    nc.tensor.matmul(ps_l1[h // 2][:, h % 2, 0:P], w1_dense[:, h * P:(h + 1) * P],
                                     early[:, 0, bass.ts(c, P)], start=(h % 2 == 0), stop=False,
                                     skip_group_check=True)
                pe.wait_ge(pairs_dve, (c + 1) * TILES)
                pe.wait_ge(pairs_act, (c + 1) * TILES)
                for h in range(NC1):
                    for k in range(CHUNKS):
                        last = nc.tensor.matmul(ps_l1[h // 2][:, h % 2, 0:P], w1_pairs[:, k, h * P:(h + 1) * P],
                                                pairs[:, k, :], start=False, stop=(k == CHUNKS - 1),
                                                skip_group_check=True)
                    if h % 2 == 1:
                        last.then_inc(l1_done, 1)
                nc.tensor.matmul(ps_l2, ones[:], b2[:], start=True, stop=False)
                for h in range(NC1):
                    if h == 0:
                        pe.wait_ge(hid1_act, c + 1)
                    if h == 2:
                        pe.wait_ge(hid1_dve, c + 1)
                    last = nc.tensor.matmul(ps_l2, hid1_t[:, h, :], w2[:, h, :], start=False, stop=(h == NC1 - 1))
                last.then_inc(l2_done, 1)

            for i in range(SEL):
                pe.wait_ge(hi_done, i + 1)
                pe.wait_ge(lo_done, i + 1)
                pe.wait_ge(onehot_done, i + 1)
                if i >= 4:
                    pe.wait_ge(sel_done, i - 3)
                for k in range(KSEL):
                    for part in (tbl_hi, tbl_lo):
                        last = nc.tensor.matmul(ps_sel[i % 4], part[i % 2][:, k, :], onehot[i % 2][:, k, :],
                                                start=(k == 0 and part is tbl_hi),
                                                stop=(k == KSEL - 1 and part is tbl_lo))
                last.then_inc(early_psum, 1)
                if i == 0:
                    pe.wait_ge(ident_in, 16)
                if 1 <= i <= NGRP:
                    if i >= 3:
                        pe.wait_ge(feat_act, i - 2)
                    transposes(0, i - 1)
            for i in range(max(SEL - 1, 0), NGRP):
                pe.wait_ge(feat_act, i - 1)
                transposes(0, i)
            pe.wait_ge(dense_in, 16)
            pe.wait_ge(w1_dense_sum, 1)
            pe.wait_ge(w1_in, 16)
            pe.wait_ge(w2_in, 32)
            pe.wait_ge(ones_set, 1)
            with pe.Fori(0, BLOCKS - 1) as c:
                gram_and_mlp(c)
                for i in range(NGRP):
                    if i >= 2 and i % 2 == 0:
                        pe.wait_ge(feat_dve, c * DVE_GRPS + (1 + i // 2))
                    elif i >= 2:
                        pe.wait_ge(feat_act, c * ACT_GRPS + (NGRP + i // 2))
                    transposes(c + 1, i)
            gram_and_mlp(BLOCKS - 1)

        @block.scalar
        def _(act):
            def early_slots(block_no):
                nc.scalar.copy(feat_t[:, :, 0:EARLY].rearrange("d s f -> d f s"),
                               early[:, :, bass.ts(block_no, P)]).then_inc(early_feat, 1)

            def gathered_slots(block_no, i):
                g, n = EARLY + GROUPS[i][0], len(GROUPS[i])
                act.wait_ge(tr_done, block_no * NGRP + (i + 1))
                nc.scalar.copy(feat_t[:, :, g:g + n].rearrange("d s f -> d f s"),
                               ps_tr[i % 2][:, 0:n, :]).then_inc(feat_act, 1)

            def pairs_and_hidden1(c):
                for tile in range(TILES):
                    act.wait_ge(gram_done, c * TILES + (tile + 1))
                    pairs_out(nc.scalar.copy, tile, (0, 1)).then_inc(pairs_act, 1)
                act.wait_ge(l1_done, c * 2 + 1)
                for h in range(2):
                    last = nc.scalar.activation(hid1_t[:, h, :], ps_l1[0][:, h, 0:P], ACT.Relu, bias=b1[:, h:h + 1])
                last.then_inc(hid1_act, 1)

            for i in range(SEL):
                act.wait_ge(sel_tbl_in[i], 16)
                if i >= 2:
                    act.wait_ge(early_psum, i - 1)
                nc.scalar.copy(tbl_hi[i % 2][:], sel_tbl[i][:]).then_inc(hi_done, 1)
                if i >= 1:
                    act.wait_ge(early_psum, i)
                    nc.scalar.copy(early[:, i, :], ps_sel[(i - 1) % 4]).then_inc(sel_done, 1)
                if 2 <= i <= NGRP:
                    gathered_slots(0, i - 2)
            act.wait_ge(early_psum, SEL)
            nc.scalar.copy(early[:, SEL, :], ps_sel[(SEL - 1) % 4]).then_inc(sel_done, 1)
            for i in range(max(SEL - 2, 0), NGRP):
                gathered_slots(0, i)
            act.wait_ge(sel_done, SEL)
            act.wait_ge(dense_in, 16)
            early_slots(0)
            act.wait_ge(b1_in, 16)
            with act.Fori(0, BLOCKS - 1) as c:
                pairs_and_hidden1(c)
                early_slots(c + 1)
                for i in range(1, NGRP, 2):
                    gathered_slots(c + 1, i)
            pairs_and_hidden1(BLOCKS - 1)

        @block.vector
        def _(dve):
            def pairs_to_y(c):
                for tile in range(TILES):
                    dve.wait_ge(gram_done, c * TILES + (tile + 1))
                    pairs_out(nc.vector.tensor_copy, tile, (2, 3)).then_inc(pairs_dve, 1)
                dve.wait_ge(l1_done, c * 2 + 2)
                for h in range(2, 4):
                    last = nc.vector.tensor_scalar(hid1_t[:, h, :], ps_l1[1][:, h % 2, 0:P], b1[:, h:h + 1], 0.0,
                                                   ALU.add, ALU.max)
                last.then_inc(hid1_dve, 1)
                dve.wait_ge(l2_done, c + 1)
                nc.vector.scalar_tensor_tensor(out=hid2[:], in0=ps_l2, scalar=0.0, in1=w3[:], op0=ALU.max,
                                               op1=ALU.mult, accum_out=y[:, bass.ts(c, 1)]).then_inc(y_done, 1)

            nc.vector.memset(ones[:], 1.0).then_inc(ones_set, 1)
            dve.wait_ge(row_id_in, 16)
            for i in range(SEL):
                dve.wait_ge(sel_ids_in[min(i, 1)], 16)
                if i >= 2:
                    dve.wait_ge(early_psum, i - 1)
                for k in range(KSEL):
                    last = nc.vector.tensor_scalar(onehot[i % 2][:, k, :], sel_ids[:, i, :], row_id[:, k:k + 1],
                                                   None, ALU.is_equal)
                last.then_inc(onehot_done, 1)
                dve.wait_ge(hi_done, i + 1)
                nc.vector.tensor_tensor(tbl_lo[i % 2][:], sel_tbl[i][:], tbl_hi[i % 2][:].bitcast(F32),
                                        ALU.subtract).then_inc(lo_done, 1)
            nc.vector.memset(feat_t[:, :, SLOTS:PAD], 0.0).then_inc(feat_dve, 1)
            dve.wait_ge(w1_dense_in, 16)
            nc.vector.tensor_tensor(w1_dense[:], w1_dense2[:, 0, :], w1_dense2[:, 1, :],
                                    ALU.add).then_inc(w1_dense_sum, 1)
            dve.wait_ge(b1_in, 16)
            dve.wait_ge(w3_in, 16)
            with dve.Fori(0, BLOCKS - 1) as c:
                pairs_to_y(c)
                for i in range(0, NGRP, 2):
                    g, n = EARLY + GROUPS[i][0], len(GROUPS[i])
                    dve.wait_ge(tr_done, c * NGRP + (NGRP + i + 1))
                    nc.vector.tensor_copy(feat_t[:, :, g:g + n].rearrange("d s f -> d f s"),
                                          ps_tr[0][:, 0:n, :]).then_inc(feat_dve, 1)
            pairs_to_y(BLOCKS - 1)


def kernel(**inputs):
    import numpy as np
    import concourse.bacc as bacc
    from concourse.bass_utils import run_bass_kernel_spmd

    nc = bacc.Bacc("TRN2", target_bir_lowering=False, num_devices=1)
    arrays = {}

    def give(name, a):
        name = "in_" + name
        arrays[name] = np.ascontiguousarray(a)
        return nc.dram_tensor(name, arrays[name].shape, mybir.dt.from_np(arrays[name].dtype),
                              kind="ExternalInput").ap()

    ids = np.asarray(inputs["ids"])
    dense = np.asarray(inputs["r_dense_features"])
    w1 = np.asarray(inputs["W_top1"])
    slot_feature = [0] + [1 + t for t in SELECTED] + [1 + t for t in GATHERED]
    tri_i, tri_j = np.triu_indices(SLOTS, k=1)
    pair_row = {(int(i), int(j)): D + n for n, (i, j) in enumerate(zip(tri_i, tri_j))}
    w1_pairs = np.zeros((P, CHUNKS, HID1), w1.dtype)
    for g in range(1, SLOTS):
        for f in range(g):
            i, j = sorted((slot_feature[f], slot_feature[g]))
            w1_pairs[32 * (g % Q) + f, g // Q] = w1[pair_row[i, j]]
    sel_tbl = np.zeros((SEL, SEL_ROWS, D), np.float32)
    for n, t in enumerate(SELECTED):
        sel_tbl[n, :inputs[f"tbl_{t}"].shape[0]] = np.asarray(inputs[f"tbl_{t}"])

    args = [
        give("idx", ids[:, list(GATHERED)].reshape(BLOCKS, P, NG).transpose(1, 0, 2)),
        give("sel_ids", ids[:, list(SELECTED)].T),
        give("row_id", np.arange(SEL_ROWS, dtype=np.float32).reshape(P, KSEL)),
        give("ident", np.eye(P, dtype=np.float32)),
        give("dense_t", dense.T),
        give("sel_tbl", sel_tbl.reshape(SEL, P, KSEL, D)),
        [give(f"tbl_{t}", inputs[f"tbl_{t}"]) for t in GATHERED],
        give("w1_pairs", w1_pairs),
        give("w1_dense", np.stack([w1[:D], w1[-D:]], axis=1)),
        give("b1", np.asarray(inputs["b_top1"]).reshape(NC1, P).T),
        give("w2", np.asarray(inputs["W_top2"]).reshape(NC1, P, HID2).transpose(1, 0, 2)),
        give("b2", np.asarray(inputs["b_top2"]).reshape(1, HID2)),
        give("w3", np.asarray(inputs["W_top3"]).reshape(HID2)),
    ]
    y = nc.dram_tensor("out_y", (P, BLOCKS), F32, kind="ExternalOutput").ap()
    build(nc, *args, y)
    result = run_bass_kernel_spmd(nc, [arrays], core_ids=[0])
    return np.asarray(result.results[0]["out_y"]).T.reshape(BATCH, 1)
```

```python
from contextlib import ExitStack

import concourse.bass as bass
from concourse import mybir

F32 = mybir.dt.float32
F32R = mybir.dt.float32r
I32 = mybir.dt.int32
ALU = mybir.AluOpType
ACT = mybir.ActivationFunctionType

P = 128
D = 128
BATCH = 512
BLOCKS = BATCH // P
TABLES = 26
SLOTS = TABLES + 1
PAD = 32
Q = 4
LOW = 3
CHUNKS = (SLOTS - LOW) // Q
assert CHUNKS * Q == SLOTS - LOW and SLOTS + LOW - 1 <= PAD
GCOLS = SLOTS
HID1, HID2 = 512, 256
NC1 = HID1 // P

SELECTED = (2, 6, 7, 8)
GATHERED = tuple(t for t in range(TABLES) if t not in SELECTED)
SEL = len(SELECTED)
EARLY = SEL + 1
SEL_ROWS = 1024
KSEL = SEL_ROWS // P
K_DVE = KSEL - 1
NG = len(GATHERED)
QUARTERS = 4
QS = P // QUARTERS
PER_TILE = QS // Q
TILES = QUARTERS
PER_DMA = P // QS
REST = NG % PER_DMA


def gather_plan():
    whole = NG - REST
    plan = []
    for quarter in range(QUARTERS):
        s = quarter * QS
        gathers = []
        if quarter == 0 and REST % 2:
            gathers.append((NG - 1, 1, s, P))
        if quarter % 2 == 0 and REST >= 2:
            gathers.append((whole, 2, s, 2 * QS))
        gathers += [(t, PER_DMA, s, QS) for t in range(0, whole, PER_DMA)]
        first = (len(gathers) + 1) // 2
        plan += [gathers[:first], gathers[first:]]
    return plan


def merged(gathers):
    out = []
    for m, (t, n, s, ns) in enumerate(gathers):
        if out and out[-1][3:] == (n, s, ns) and out[-1][2] + n * out[-1][1] == t:
            out[-1] = (out[-1][0], out[-1][1] + 1, *out[-1][2:])
        else:
            out.append((m, 1, t, n, s, ns))
    return out


PLAN = gather_plan()
NGRP = len(PLAN)
assert NGRP == 2 * QUARTERS and max(map(len, PLAN)) <= 4
HALF_GRPS = QUARTERS
GATHERS = sum(len(group) for group in PLAN)
FIRST_GATHER = [sum(len(group) for group in PLAN[:i]) for i in range(NGRP)]


def build(nc, ids_d, base_d, sel_ids_d, row_id_d, ident_d, dense_t_d, sel_tbl_d, tables_d,
          w1_pairs_d, w1_dense_d, b1_d, w2_d, b2_d, w3_d, y_d):
    ctx = ExitStack()
    with ctx:
        def sb(name, shape, dt=F32):
            return ctx.enter_context(nc.sbuf_tensor(name, shape, dt))

        def ps(name, shape):
            return ctx.enter_context(nc.psum_tensor(name, shape, F32))

        def sem(name):
            return ctx.enter_context(nc.semaphore(name))

        ids = sb("ids", [P, BLOCKS * GATHERS], I32)
        base = sb("base", [P, BLOCKS * GATHERS], I32)
        idx = sb("idx", [P, BLOCKS * GATHERS], I32)
        sel_ids = sb("sel_ids", [P, SEL, BATCH], I32)
        row_id = sb("row_id", [P, KSEL])
        ident = sb("ident", [P, P])
        sel_tbl = [sb(f"sel_tbl{i}", [P, KSEL, D]) for i in range(SEL)]
        tbl_hi = [sb(f"tbl_hi{i}", [P, KSEL, D], F32R) for i in range(2)]
        tbl_lo = [sb(f"tbl_lo{i}", [P, KSEL, D], F32R) for i in range(2)]
        onehot = [sb(f"onehot{i}", [P, KSEL, BATCH], F32R) for i in range(2)]
        early = sb("early", [P, EARLY, BATCH])
        rows = sb("rows", [P, GATHERS, D])
        feat_t = sb("feat_t", [P, P, PAD])
        pairs = sb("pairs", [P, CHUNKS, P])
        w1_pairs = sb("w1_pairs", [P, CHUNKS, HID1])
        w1_dense2 = sb("w1_dense2", [P, 2, HID1])
        w1_dense = sb("w1_dense", [P, HID1])
        b1 = sb("b1", [P, NC1])
        w2 = sb("w2", [P, NC1, HID2])
        b2 = sb("b2", [P, HID2])
        w3 = sb("w3", [P, HID2])
        hid1_t = sb("hid1_t", [P, NC1, P])
        hid2 = sb("hid2", [P, HID2])
        hid2_w3 = sb("hid2_w3", [P, HID2])
        distance = sb("distance", [P, BATCH])
        y = sb("y", [P, BLOCKS])

        ps_tr = [ps(f"ps_tr{i}", [P, 4, P]) for i in range(2)]
        ps_gram = [ps(f"ps_gram{i}", [P, 2, 512]) for i in range(2)]
        ps_l1 = [ps(f"ps_l1{i}", [P, 2, 256]) for i in range(2)]
        ps_sel = [ps_gram[i // 2][:, i % 2, :] for i in range(4)]
        ps_l2 = ps_gram[0][:, 0, 0:HID2]

        ids_in = sem("ids_in")
        idx_ready = sem("idx_ready")
        row_id_in = sem("row_id_in")
        sel_ids_in = [sem(f"sel_ids_in{i}") for i in range(2)]
        sel_tbl_in = [sem(f"sel_tbl_in{i}") for i in range(SEL)]
        ident_in = sem("ident_in")
        dense_in = sem("dense_in")
        w1_dense_in = sem("w1_dense_in")
        w1_in = sem("w1_in")
        w2_in = sem("w2_in")
        b1_in = sem("b1_in")
        w3_in = sem("w3_in")
        rows_in = [sem(f"rows_in{i}") for i in range(NGRP)]
        low_slots = sem("low_slots")
        pairs_zero = sem("pairs_zero")
        below_dve = sem("below_dve")
        below_act = sem("below_act")
        hid2_biased = sem("hid2_biased")
        distance_done = sem("distance_done")
        w1_dense_sum = sem("w1_dense_sum")
        hi_done = sem("hi_done")
        lo_done = sem("lo_done")
        onehot_dve = sem("onehot_dve")
        onehot_act = sem("onehot_act")
        sel_done = sem("sel_done")
        early_psum = sem("early_psum")
        early_feat = sem("early_feat")
        tr_done = sem("tr_done")
        feat_dve = sem("feat_dve")
        feat_act = sem("feat_act")
        gram_done = sem("gram_done")
        pairs_dve = sem("pairs_dve")
        pairs_act = sem("pairs_act")
        l1_done = sem("l1_done")
        hid1_act = sem("hid1_act")
        hid1_dve = sem("hid1_dve")
        l2_done = sem("l2_done")
        y_done = sem("y_done")
        out_done = sem("out_done")

        block = ctx.enter_context(nc.Block())

        def pairs_out(engine, copy, tile, quads, below, below_count):
            src = ps_gram[tile % 2][:, :, 0:PER_TILE // 2 * Q * GCOLS].rearrange(
                "p h (n j g) -> p h n j g", n=PER_TILE // 2, j=Q)
            own = src[:, :, :, :, LOW:SLOTS].rearrange("p h n j (k q) -> p h n j k q", q=Q)
            dst = pairs[:, :, tile * QS:(tile + 1) * QS].rearrange("p k (h n j) -> p h n j k", h=2, j=Q)
            for j in quads:
                last = copy(dst[96:128, :, :, j, CHUNKS - 2:CHUNKS], src[32 * j:32 * j + 32, :, :, j, 0:2])
            last.then_inc(below, 1)
            for q in range(Q):
                if q == Q - 1:
                    engine.wait_ge(below, below_count)
                for j in quads:
                    last = copy(dst[32 * q:32 * q + SLOTS, :, :, j, :],
                                own[32 * j:32 * j + SLOTS, :, :, j, :, q])
            return last

        @block.sync
        def _(sp):
            sp.dma_start(ids[:], ids_d).then_inc(ids_in, 16)
            sp.dma_start(base[:], base_d).then_inc(ids_in, 16)
            sp.dma_start(sel_ids[:, 0, :], sel_ids_d[0, :].partition_broadcast(P)).then_inc(sel_ids_in[0], 16)
            sp.dma_start(row_id[:], row_id_d).then_inc(row_id_in, 16)
            sp.dma_start(sel_tbl[0][:], sel_tbl_d[0]).then_inc(sel_tbl_in[0], 16)
            sp.dma_start(sel_ids[:, 1:SEL, :].rearrange("p t b -> p (t b)"),
                         sel_ids_d[1:SEL, :].rearrange("t b -> (t b)").partition_broadcast(P)
                         ).then_inc(sel_ids_in[1], 16)
            for i in range(1, SEL):
                sp.dma_start(sel_tbl[i][:], sel_tbl_d[i]).then_inc(sel_tbl_in[i], 16)
            sp.dma_start(early[:, 0, :], dense_t_d).then_inc(dense_in, 16)
            sp.dma_start(ident[:], ident_d).then_inc(ident_in, 16)
            sp.dma_start(w1_dense2[:], w1_dense_d).then_inc(w1_dense_in, 16)
            sp.dma_start(w1_pairs[:], w1_pairs_d).then_inc(w1_in, 16)
            sp.dma_start(b1[:], b1_d).then_inc(b1_in, 16)
            sp.dma_start(w2[:], w2_d).then_inc(w2_in, 16)
            sp.dma_start(b2[:], b2_d.partition_broadcast(P)).then_inc(w3_in, 16)
            sp.dma_start(w3[:], w3_d.partition_broadcast(P)).then_inc(w3_in, 16)
            sp.wait_ge(y_done, BLOCKS)
            sp.dma_start(y_d, y[:]).then_inc(out_done, 16)
            sp.wait_ge(out_done, 16)

        def feat_out(copy, i):
            for m, count, t0, n, s0, ns in merged(PLAN[i]):
                g = EARLY + t0
                last = copy(feat_t[:, s0:s0 + ns, g:g + n * count].rearrange("d s f -> d f s"),
                            ps_tr[i % 2][:, m:m + count, :].rearrange("d m (f s) -> d (m f) s", f=n))
            return last

        @block.gpsimd
        def _(pool):
            pool.wait_ge(ids_in, 32)
            nc.gpsimd.tensor_tensor(idx[:], ids[:], base[:], ALU.add).then_inc(idx_ready, 1)
            pool.wait_ge(idx_ready, 1)
            for c in range(BLOCKS):
                for i, gathers in enumerate(PLAN):
                    if c >= 1:
                        pool.wait_ge(tr_done, (c - 1) * NGRP + i + 1)
                    for n in range(FIRST_GATHER[i], FIRST_GATHER[i] + len(gathers)):
                        col = c * GATHERS + n
                        pool.indirect_dma_start(
                            out=rows[:, n, :], out_offset=None, in_=tables_d,
                            in_offset=bass.IndirectOffsetOnAxis(ap=idx[:, col:col + 1], axis=0),
                        ).then_inc(rows_in[i], 16)

        @block.tensor
        def _(pe):
            def transposes(c, quarter):
                for i in (2 * quarter, 2 * quarter + 1):
                    pe.wait_ge(rows_in[i], (c + 1) * (16 * len(PLAN[i])))
                    if i % 2 == 0:
                        pe.wait_ge(feat_dve, c * HALF_GRPS + (1 + quarter))
                    elif quarter >= 1:
                        pe.wait_ge(feat_act, c * HALF_GRPS + quarter)
                    for m in range(len(PLAN[i])):
                        last = nc.tensor.transpose(ps_tr[i % 2][:, m, :], rows[:, FIRST_GATHER[i] + m, :], ident[:])
                    last.then_inc(tr_done, 1)

            def gram(c, tile):
                pe.wait_ge(feat_dve, c * HALF_GRPS + (tile + 2))
                pe.wait_ge(feat_act, c * HALF_GRPS + (tile + 1))
                if tile == 0:
                    pe.wait_ge(early_feat, c + 1)
                if tile >= 2:
                    pe.wait_ge(pairs_dve, c * TILES + (tile - 1))
                    pe.wait_ge(pairs_act, c * TILES + (tile - 1))
                for n in range(PER_TILE):
                    s = tile * QS + n * Q
                    half, m = divmod(n, PER_TILE // 2)
                    last = nc.tensor.matmul(
                        ps_gram[tile % 2][:, half, m * Q * GCOLS:(m + 1) * Q * GCOLS],
                        feat_t[:, s:s + Q, :].rearrange("d s f -> d (s f)"),
                        feat_t[:, s:s + Q, 0:GCOLS], start=True, stop=True)
                last.then_inc(gram_done, 1)

            def hidden1_dense(c):
                for h in range(NC1):
                    nc.tensor.matmul(ps_l1[h // 2][:, h % 2, 0:P], w1_dense[:, h * P:(h + 1) * P],
                                     early[:, 0, bass.ts(c, P)], start=(h % 2 == 0), stop=False,
                                     skip_group_check=True)

            def hidden1_pairs(c):
                pe.wait_ge(pairs_dve, (c + 1) * TILES)
                pe.wait_ge(pairs_act, (c + 1) * TILES)
                for h in range(NC1):
                    for k in range(CHUNKS):
                        last = nc.tensor.matmul(ps_l1[h // 2][:, h % 2, 0:P], w1_pairs[:, k, h * P:(h + 1) * P],
                                                pairs[:, k, :], start=False, stop=(k == CHUNKS - 1),
                                                skip_group_check=True)
                    if h % 2 == 1:
                        last.then_inc(l1_done, 1)

            def hidden2(c):
                for h in range(NC1):
                    if h == 0:
                        pe.wait_ge(hid1_act, c + 1)
                    if h == 2:
                        pe.wait_ge(hid1_dve, c + 1)
                    last = nc.tensor.matmul(ps_l2, hid1_t[:, h, :], w2[:, h, :], start=(h == 0), stop=(h == NC1 - 1))
                last.then_inc(l2_done, 1)

            for i in range(SEL):
                pe.wait_ge(hi_done, i + 1)
                if i >= 4:
                    pe.wait_ge(sel_done, i - 3)
                for k in range(KSEL):
                    if k < K_DVE:
                        pe.wait_ge(onehot_dve, i * K_DVE + k + 1)
                    else:
                        pe.wait_ge(onehot_act, i * (KSEL - K_DVE) + k - K_DVE + 1)
                    nc.tensor.matmul(ps_sel[i % 4], tbl_hi[i % 2][:, k, :], onehot[i % 2][:, k, :],
                                     start=(k == 0), stop=False)
                pe.wait_ge(lo_done, i + 1)
                for k in range(KSEL):
                    last = nc.tensor.matmul(ps_sel[i % 4], tbl_lo[i % 2][:, k, :], onehot[i % 2][:, k, :],
                                            start=False, stop=(k == KSEL - 1))
                last.then_inc(early_psum, 1)
            pe.wait_ge(ident_in, 16)
            pe.wait_ge(dense_in, 16)
            pe.wait_ge(w1_dense_sum, 1)
            pe.wait_ge(w1_in, 16)
            pe.wait_ge(w2_in, 16)
            def second_half(c):
                transposes(c, 2)
                gram(c, 1)
                gram(c, 2)
                transposes(c, 3)
                hidden1_dense(c)
                gram(c, 3)

            transposes(0, 0)
            transposes(0, 1)
            gram(0, 0)
            with pe.Fori(0, BLOCKS - 1) as c:
                second_half(c)
                transposes(c + 1, 0)
                hidden1_pairs(c)
                transposes(c + 1, 1)
                hidden2(c)
                pe.wait_ge(y_done, c + 1)
                gram(c + 1, 0)
            second_half(BLOCKS - 1)
            hidden1_pairs(BLOCKS - 1)
            hidden2(BLOCKS - 1)

        @block.scalar
        def _(act):
            for i in range(SEL):
                act.wait_ge(sel_tbl_in[i], 16)
                if i >= 2:
                    act.wait_ge(early_psum, i - 1)
                nc.scalar.copy(tbl_hi[i % 2][:], sel_tbl[i][:]).then_inc(hi_done, 1)
                act.wait_ge(row_id_in, 16)
                act.wait_ge(sel_ids_in[min(i, 1)], 16)
                for k in range(K_DVE, KSEL):
                    n = i * (KSEL - K_DVE) + k - K_DVE
                    if n >= 1:
                        act.wait_ge(onehot_act, n)
                    nc.scalar.activation(distance[:], sel_ids[:, i, :], ACT.Abs, bias=row_id[:, k:k + 1],
                                         scale=-1.0).then_inc(distance_done, 1)
                    act.wait_ge(distance_done, n + 1)
                    nc.scalar.activation(onehot[i % 2][:, k, :], distance[:], ACT.Relu, bias=1.0,
                                         scale=-1.0).then_inc(onehot_act, 1)
                if i >= 1:
                    act.wait_ge(early_psum, i)
                    nc.scalar.copy(early[:, i, :], ps_sel[(i - 1) % 4]).then_inc(sel_done, 1)
            act.wait_ge(early_psum, SEL)
            nc.scalar.copy(early[:, SEL, :], ps_sel[(SEL - 1) % 4]).then_inc(sel_done, 1)
            act.wait_ge(sel_done, SEL)
            act.wait_ge(dense_in, 16)
            act.wait_ge(b1_in, 16)

            def early_slots(c):
                nc.scalar.copy(feat_t[:, :, SLOTS:SLOTS + LOW - 1].rearrange("d s f -> d f s"),
                               early[:, 1:LOW, bass.ts(c, P)])
                nc.scalar.copy(feat_t[:, :, 0:EARLY].rearrange("d s f -> d f s"),
                               early[:, :, bass.ts(c, P)]).then_inc(early_feat, 1)

            def gathered_slots(c, quarter):
                for i in (2 * quarter, 2 * quarter + 1):
                    if i % 2 == 1:
                        act.wait_ge(tr_done, c * NGRP + (i + 1))
                        feat_out(nc.scalar.copy, i).then_inc(feat_act, 1)

            def interactions(c, tile):
                act.wait_ge(gram_done, c * TILES + (tile + 1))
                pairs_out(act, nc.scalar.copy, tile, (0, 1), below_act, c * TILES + (tile + 1)).then_inc(pairs_act, 1)

            def second_half(c):
                gathered_slots(c, 2)
                interactions(c, 1)
                gathered_slots(c, 3)
                interactions(c, 2)
                interactions(c, 3)

            def hidden1(c):
                act.wait_ge(l1_done, c * 2 + 1)
                for h in range(2):
                    last = nc.scalar.activation(hid1_t[:, h, :], ps_l1[0][:, h, 0:P], ACT.Relu, bias=b1[:, h:h + 1])
                last.then_inc(hid1_act, 1)

            act.wait_ge(pairs_zero, 1)
            act.wait_ge(feat_dve, 1)
            early_slots(0)
            gathered_slots(0, 0)
            gathered_slots(0, 1)
            interactions(0, 0)
            with act.Fori(0, BLOCKS - 1) as c:
                second_half(c)
                early_slots(c + 1)
                gathered_slots(c + 1, 0)
                hidden1(c)
                gathered_slots(c + 1, 1)
                interactions(c + 1, 0)
            second_half(BLOCKS - 1)
            hidden1(BLOCKS - 1)

        @block.vector
        def _(dve):
            dve.wait_ge(row_id_in, 16)
            for i in range(SEL):
                dve.wait_ge(sel_ids_in[min(i, 1)], 16)
                if i >= 2:
                    dve.wait_ge(early_psum, i - 1)
                for k in range(K_DVE):
                    nc.vector.tensor_scalar(onehot[i % 2][:, k, :], sel_ids[:, i, :], row_id[:, k:k + 1],
                                            None, ALU.is_equal).then_inc(onehot_dve, 1)
                dve.wait_ge(hi_done, i + 1)
                nc.vector.tensor_tensor(tbl_lo[i % 2][:], sel_tbl[i][:], tbl_hi[i % 2][:].bitcast(F32),
                                        ALU.subtract).then_inc(lo_done, 1)
            nc.vector.memset(feat_t[:, :, SLOTS + LOW - 1:PAD], 0.0).then_inc(feat_dve, 1)
            nc.vector.memset(pairs[:], 0.0).then_inc(pairs_zero, 1)
            dve.wait_ge(pairs_zero, 1)
            dve.wait_ge(w1_dense_in, 16)
            nc.vector.tensor_tensor(w1_dense[:], w1_dense2[:, 0, :], w1_dense2[:, 1, :],
                                    ALU.add).then_inc(w1_dense_sum, 1)
            dve.wait_ge(b1_in, 16)
            dve.wait_ge(w3_in, 32)

            def gathered_slots(c, quarter):
                for i in (2 * quarter, 2 * quarter + 1):
                    if i % 2 == 0:
                        dve.wait_ge(tr_done, c * NGRP + (i + 1))
                        feat_out(nc.vector.tensor_copy, i).then_inc(feat_dve, 1)

            def interactions(c, tile):
                dve.wait_ge(gram_done, c * TILES + (tile + 1))
                pairs_out(dve, nc.vector.tensor_copy, tile, (2, 3), below_dve, c * TILES + (tile + 1)).then_inc(pairs_dve, 1)

            def second_half(c):
                gathered_slots(c, 2)
                interactions(c, 1)
                gathered_slots(c, 3)
                interactions(c, 2)
                interactions(c, 3)

            def hidden1(c):
                dve.wait_ge(l1_done, c * 2 + 2)
                for h in range(2, 4):
                    last = nc.vector.tensor_scalar(hid1_t[:, h, :], ps_l1[1][:, h % 2, 0:P], b1[:, h:h + 1], 0.0,
                                                   ALU.add, ALU.max)
                last.then_inc(hid1_dve, 1)

            def output(c):
                dve.wait_ge(l2_done, c + 1)
                nc.vector.tensor_tensor(hid2[:], ps_l2, b2[:], ALU.add).then_inc(hid2_biased, 1)
                dve.wait_ge(hid2_biased, c + 1)
                nc.vector.scalar_tensor_tensor(out=hid2_w3[:], in0=hid2[:], scalar=0.0, in1=w3[:], op0=ALU.max,
                                               op1=ALU.mult, accum_out=y[:, bass.ts(c, 1)]).then_inc(y_done, 1)

            gathered_slots(0, 0)
            gathered_slots(0, 1)
            interactions(0, 0)
            with dve.Fori(0, BLOCKS - 1) as c:
                second_half(c)
                gathered_slots(c + 1, 0)
                hidden1(c)
                gathered_slots(c + 1, 1)
                output(c)
                interactions(c + 1, 0)
            second_half(BLOCKS - 1)
            hidden1(BLOCKS - 1)
            output(BLOCKS - 1)


def kernel(**inputs):
    import numpy as np
    import concourse.bacc as bacc
    from concourse.bass_utils import run_bass_kernel_spmd

    nc = bacc.Bacc("TRN2", target_bir_lowering=False, num_devices=1)
    arrays = {}

    def give(name, a):
        name = "in_" + name
        arrays[name] = np.ascontiguousarray(a)
        return nc.dram_tensor(name, arrays[name].shape, mybir.dt.from_np(arrays[name].dtype),
                              kind="ExternalInput").ap()

    ids = np.asarray(inputs["ids"])
    dense = np.asarray(inputs["r_dense_features"])
    w1 = np.asarray(inputs["W_top1"])
    slot_feature = [0] + [1 + t for t in SELECTED] + [1 + t for t in GATHERED]
    tri_i, tri_j = np.triu_indices(SLOTS, k=1)
    pair_row = {(int(i), int(j)): D + n for n, (i, j) in enumerate(zip(tri_i, tri_j))}
    w1_pairs = np.zeros((P, CHUNKS, HID1), w1.dtype)
    places = {(f, g): (PAD * ((g - LOW) % Q) + f, (g - LOW) // Q) for g in range(LOW, SLOTS) for f in range(g)}
    for f in range(LOW - 1):
        for g in range(f + 1, LOW):
            places[f, g] = (PAD * (Q - 1) + SLOTS + g - 1, CHUNKS - 2 + f)
    for (f, g), (row, chunk) in places.items():
        i, j = sorted((slot_feature[f], slot_feature[g]))
        w1_pairs[row, chunk] = w1[pair_row[i, j]]
    sel_tbl = np.zeros((SEL, SEL_ROWS, D), np.float32)
    for n, t in enumerate(SELECTED):
        sel_tbl[n, :inputs[f"tbl_{t}"].shape[0]] = np.asarray(inputs[f"tbl_{t}"])

    tbl_rows = [inputs[f"tbl_{t}"].shape[0] for t in GATHERED]
    first_row = np.concatenate([[0], np.cumsum(tbl_rows)[:-1]]).astype(np.int32)
    ids_cols, base_cols = [], []
    for c in range(BLOCKS):
        for gathers in PLAN:
            for t0, n, s0, ns in gathers:
                samples = slice(c * P + s0, c * P + s0 + ns)
                ids_cols.append(np.concatenate([ids[samples, GATHERED[t]] for t in range(t0, t0 + n)]))
                base_cols.append(np.repeat(first_row[t0:t0 + n], ns))

    args = [
        give("ids", np.stack(ids_cols, axis=1)),
        give("base", np.stack(base_cols, axis=1)),
        give("sel_ids", ids[:, list(SELECTED)].T),
        give("row_id", np.arange(SEL_ROWS, dtype=np.float32).reshape(P, KSEL)),
        give("ident", np.eye(P, dtype=np.float32)),
        give("dense_t", dense.T),
        give("sel_tbl", sel_tbl.reshape(SEL, P, KSEL, D)),
        give("tables", np.concatenate([np.asarray(inputs[f"tbl_{t}"]) for t in GATHERED])),
        give("w1_pairs", w1_pairs),
        give("w1_dense", np.stack([w1[:D], w1[-D:]], axis=1)),
        give("b1", np.asarray(inputs["b_top1"]).reshape(NC1, P).T),
        give("w2", np.asarray(inputs["W_top2"]).reshape(NC1, P, HID2).transpose(1, 0, 2)),
        give("b2", np.asarray(inputs["b_top2"])),
        give("w3", np.asarray(inputs["W_top3"]).reshape(HID2)),
    ]
    y = nc.dram_tensor("out_y", (P, BLOCKS), F32, kind="ExternalOutput").ap()
    build(nc, *args, y)
    result = run_bass_kernel_spmd(nc, [arrays], core_ids=[0])
    return np.asarray(result.results[0]["out_y"]).T.reshape(BATCH, 1)
```

```python
from contextlib import ExitStack

import concourse.bass as bass
from concourse import mybir

F32 = mybir.dt.float32
F32R = mybir.dt.float32r
I32 = mybir.dt.int32
ALU = mybir.AluOpType
ACT = mybir.ActivationFunctionType

P = 128
D = 128
BATCH = 512
BLOCKS = BATCH // P
LAST = BLOCKS - 1
TABLES = 26
SLOTS = TABLES + 1
PAD = 32
REPEATED = PAD - SLOTS
Q = 4
QUADRANTS = (
    (22, slice(6, 13, 2), slice(21, 25)),
    (13, slice(23, 27), slice(17, 21)),
    (22, slice(5, 12, 2), slice(23, 30, 2)),
    (13, slice(22, 32, 3), slice(13, 17)),
)
CHUNKS = 4
HID1, HID2 = 512, 256
NC1 = HID1 // P

SELECTED = (2, 6, 7, 8, 10, 11, 14)
GATHERED = tuple(t for t in range(TABLES) if t not in SELECTED)
SEL = len(SELECTED)
EARLY = SEL + 1
SEL_ROWS = 1024
KSEL = SEL_ROWS // P
HALF = KSEL // 2
WARM_UP = 5
K_DVE = [KSEL - (1 if i % 3 == 0 else 2) for i in range(SEL)]
NG = len(GATHERED)
QUARTERS = 4
QS = P // QUARTERS
PER_TILE = QS // Q
TILES = QUARTERS
PER_DMA = P // QS
REST = NG % PER_DMA


def pair_places():
    slot = [*range(SLOTS), *range(REPEATED)]
    places = {}
    for q, (head, *columns) in enumerate(QUADRANTS):
        heads, tails = [range(PAD)[c] for c in columns]
        for k in range(CHUNKS):
            for row in range(PAD):
                f, g = sorted((slot[row], slot[(heads if row < head else tails)[k]]))
                if f != g:
                    places.setdefault((f, g), (PAD * q + row, k))
    assert len(places) == SLOTS * (SLOTS - 1) // 2
    return places


def gather_plan():
    whole = NG - REST
    plan = []
    for quarter in range(QUARTERS):
        s = quarter * QS
        gathers = []
        if quarter == 0 and REST % 2:
            gathers.append((NG - 1, 1, s, P))
        if quarter % 2 == 0 and REST >= 2:
            gathers.append((whole, 2, s, 2 * QS))
        gathers += [(t, PER_DMA, s, QS) for t in range(0, whole, PER_DMA)]
        first = (len(gathers) + 1) // 2
        plan += [gathers[:first], gathers[first:]]
    return plan


def merged(gathers):
    out = []
    for m, (t, n, s, ns) in enumerate(gathers):
        if out and out[-1][3:] == (n, s, ns) and out[-1][2] + n * out[-1][1] == t:
            out[-1] = (out[-1][0], out[-1][1] + 1, *out[-1][2:])
        else:
            out.append((m, 1, t, n, s, ns))
    return out


PLAN = gather_plan()
NGRP = len(PLAN)
assert NGRP == 2 * QUARTERS and max(map(len, PLAN)) <= 4
HALF_GRPS = QUARTERS
GATHERS = sum(len(group) for group in PLAN)
FIRST_GATHER = [sum(len(group) for group in PLAN[:i]) for i in range(NGRP)]


def build(nc, numbers_d, sel_ids_d, ident_d, dense_t_d, sel_tbl_d, tables_d,
          w1_pairs_d, w1_dense_d, b1_d, w2_d, b2_d, w3_d, y_d):
    ctx = ExitStack()
    with ctx:
        def sb(name, shape, dt=F32):
            return ctx.enter_context(nc.sbuf_tensor(name, shape, dt))

        def ps(name, shape):
            return ctx.enter_context(nc.psum_tensor(name, shape, F32))

        def sem(name):
            return ctx.enter_context(nc.semaphore(name))

        numbers = sb("numbers", [P, 2 * BLOCKS * GATHERS + KSEL], I32)
        ids = numbers[:, 0:BLOCKS * GATHERS]
        base = numbers[:, BLOCKS * GATHERS:2 * BLOCKS * GATHERS]
        row_number = numbers[:, 2 * BLOCKS * GATHERS:]
        idx = sb("idx", [P, BLOCKS * GATHERS], I32)
        sel_ids = sb("sel_ids", [P, SEL, BATCH], I32)
        row_id = sb("row_id", [P, KSEL])
        ident = sb("ident", [P, P])
        sel_tbl = [sb(f"sel_tbl{i}", [P, KSEL, D]) for i in range(SEL)]
        tbl_hi = [sb(f"tbl_hi{i}", [P, KSEL, D], F32R) for i in range(2)]
        tbl_lo = [sb(f"tbl_lo{i}", [P, KSEL, D], F32R) for i in range(2)]
        onehot = [sb(f"onehot{i}", [P, KSEL, BATCH], F32R) for i in range(2)]
        early = sb("early", [P, EARLY, BATCH])
        first_rows = sb("first_rows", [P, GATHERS, D])
        rows = sb("rows", [P, GATHERS, D])
        feat_t = sb("feat_t", [P, P, PAD])
        pairs = sb("pairs", [P, CHUNKS, P])
        w1_pairs = sb("w1_pairs", [P, CHUNKS, HID1])
        w1_dense2 = sb("w1_dense2", [P, 2, HID1])
        w1_dense = sb("w1_dense", [P, HID1])
        b1 = sb("b1", [P, NC1])
        w2 = sb("w2", [P, NC1, HID2])
        b2 = sb("b2", [P, HID2])
        w3 = sb("w3", [P, HID2])
        hid1_t = sb("hid1_t", [P, NC1, P])
        hid2 = sb("hid2", [P, HID2])
        hid2_w3 = sb("hid2_w3", [P, HID2])
        ones = sb("ones", [P, HID2])
        distance = sb("distance", [P, 2, BATCH])
        y = sb("y", [P, BLOCKS])

        ps_tr = [ps(f"ps_tr{i}", [P, 4, P]) for i in range(2)]
        ps_gram = [ps(f"ps_gram{i}", [P, 2, 512]) for i in range(2)]
        ps_l1 = [ps(f"ps_l1{i}", [P, 2, 256]) for i in range(2)]
        sel_bank = [i % 4 for i in range(SEL - 1)] + [3]
        ps_sel = [ps_gram[bank // 2][:, bank % 2, :] for bank in sel_bank]
        ps_l2_last = ps_tr[0][:, 0:2, :]
        ps_l2 = ps_gram[0][:, 0, 0:HID2]

        numbers_in = sem("numbers_in")
        idx_ready = sem("idx_ready")
        row_id_set = sem("row_id_set")
        sel_ids_in = [sem(f"sel_ids_in{i}") for i in range(SEL)]
        first_half_in = sem("first_half_in")
        first_half_hi = sem("first_half_hi")
        sel_tbl_in = [sem(f"sel_tbl_in{i}") for i in range(SEL)]
        ident_in = sem("ident_in")
        dense_in = sem("dense_in")
        w1_dense_in = sem("w1_dense_in")
        w1_in = sem("w1_in")
        w2_in = sem("w2_in")
        b1_in = sem("b1_in")
        w3_in = sem("w3_in")
        first_rows_in = [sem(f"first_rows_in{i}") for i in range(NGRP)]
        rows_in = [sem(f"rows_in{i}") for i in range(NGRP)]
        repeats_feat = sem("repeats_feat")
        ones_set = sem("ones_set")
        tails_dve = sem("tails_dve")
        tails_act = sem("tails_act")
        hid2_biased = sem("hid2_biased")
        distance_done = sem("distance_done")
        w1_dense_sum = sem("w1_dense_sum")
        hi_done = sem("hi_done")
        lo_done = sem("lo_done")
        onehot_dve = sem("onehot_dve")
        onehot_act = sem("onehot_act")
        sel_done = sem("sel_done")
        early_psum = sem("early_psum")
        early_feat = sem("early_feat")
        tr_done = sem("tr_done")
        feat_dve = sem("feat_dve")
        feat_act = sem("feat_act")
        gram_done = sem("gram_done")
        pairs_dve = sem("pairs_dve")
        pairs_act = sem("pairs_act")
        l1_done = sem("l1_done")
        hid1_act = sem("hid1_act")
        hid1_dve = sem("hid1_dve")
        l2_done = sem("l2_done")
        y_done = sem("y_done")
        out_done = sem("out_done")

        block = ctx.enter_context(nc.Block())

        def tile_views(tile):
            src = ps_gram[tile % 2][:].rearrange("p h (n j g) -> p h n j g", j=Q, g=PAD)
            dst = pairs[:, :, tile * QS:(tile + 1) * QS].rearrange("p k (h n j) -> p h n j k", h=2, j=Q)
            return src, dst

        def tails_out(copy, tile, quads):
            src, dst = tile_views(tile)
            for q, (_, _, tails) in enumerate(QUADRANTS):
                for j in quads:
                    last = copy(dst[PAD * q:PAD * (q + 1), :, :, j, :],
                                src[PAD * j:PAD * (j + 1), :, :, j, tails])
            return last

        def heads_out(copy, tile, quads):
            src, dst = tile_views(tile)
            for q, (head, heads, _) in enumerate(QUADRANTS):
                for j in quads:
                    last = copy(dst[PAD * q:PAD * q + head, :, :, j, :],
                                src[PAD * j:PAD * j + head, :, :, j, heads])
            return last

        @block.sync
        def _(sp):
            sp.dma_start(numbers[:], numbers_d).then_inc(numbers_in, 16)
            for i in range(SEL):
                if i == SEL - 1:
                    sp.dma_start(ident[:], ident_d).then_inc(ident_in, 16)
                sp.dma_start(sel_ids[:, i, :], sel_ids_d[i, :].partition_broadcast(P)).then_inc(sel_ids_in[i], 16)
                if i == 0:
                    sp.dma_start(sel_tbl[i][:, 0:HALF], sel_tbl_d[i][:, 0:HALF]).then_inc(first_half_in, 16)
                    sp.dma_start(sel_tbl[i][:, HALF:KSEL], sel_tbl_d[i][:, HALF:KSEL]).then_inc(sel_tbl_in[i], 16)
                else:
                    sp.dma_start(sel_tbl[i][:], sel_tbl_d[i]).then_inc(sel_tbl_in[i], 16)
            sp.dma_start(early[:, 0, :], dense_t_d).then_inc(dense_in, 16)
            sp.dma_start(w1_dense2[:], w1_dense_d).then_inc(w1_dense_in, 16)
            sp.dma_start(w1_pairs[:], w1_pairs_d).then_inc(w1_in, 16)
            sp.dma_start(b1[:], b1_d).then_inc(b1_in, 16)
            sp.dma_start(w2[:], w2_d).then_inc(w2_in, 16)
            sp.dma_start(b2[:], b2_d.partition_broadcast(P)).then_inc(w3_in, 16)
            sp.dma_start(w3[:], w3_d.partition_broadcast(P)).then_inc(w3_in, 16)
            sp.wait_ge(y_done, BLOCKS)
            sp.dma_start(y_d, y[:]).then_inc(out_done, 16)
            sp.wait_ge(out_done, 16)

        def feat_out(copy, i):
            for m, count, t0, n, s0, ns in merged(PLAN[i]):
                g = EARLY + t0
                last = copy(feat_t[:, s0:s0 + ns, g:g + n * count].rearrange("d s f -> d f s"),
                            ps_tr[i % 2][:, m:m + count, :].rearrange("d m (f s) -> d (m f) s", f=n))
            return last

        @block.gpsimd
        def _(pool):
            pool.wait_ge(numbers_in, 16)
            nc.gpsimd.tensor_tensor(idx[:], ids, base, ALU.add).then_inc(idx_ready, 1)
            pool.wait_ge(idx_ready, 1)
            for c in range(BLOCKS):
                for i, gathers in enumerate(PLAN):
                    if c >= 2:
                        pool.wait_ge(tr_done, (c - 1) * NGRP + i + 1)
                    for n in range(FIRST_GATHER[i], FIRST_GATHER[i] + len(gathers)):
                        col = c * GATHERS + n
                        pool.indirect_dma_start(
                            out=(rows if c else first_rows)[:, n, :], out_offset=None, in_=tables_d,
                            in_offset=bass.IndirectOffsetOnAxis(ap=idx[:, col:col + 1], axis=0),
                        ).then_inc((rows_in if c else first_rows_in)[i], 16)

        @block.tensor
        def _(pe):
            def transposes(c, i):
                quarter = i // 2
                first = isinstance(c, int) and c == 0
                if first:
                    pe.wait_ge(first_rows_in[i], 16 * len(PLAN[i]))
                else:
                    pe.wait_ge(rows_in[i], c * (16 * len(PLAN[i])))
                if not (first and quarter == 0):
                    pe.wait_ge(feat_dve if i % 2 else feat_act, c * HALF_GRPS + quarter)
                source = first_rows if first else rows
                for m in range(len(PLAN[i])):
                    last = nc.tensor.transpose(ps_tr[i % 2][:, m, :], source[:, FIRST_GATHER[i] + m, :], ident[:])
                last.then_inc(tr_done, 1)

            def quarter_transposes(c, quarter):
                transposes(c, 2 * quarter)
                transposes(c, 2 * quarter + 1)

            def gram(c, tile):
                if tile >= 2:
                    pe.wait_ge(pairs_dve, c * TILES + (tile - 1))
                    pe.wait_ge(pairs_act, c * TILES + (tile - 1))
                pe.wait_ge(feat_dve, c * HALF_GRPS + (tile + 1))
                pe.wait_ge(feat_act, c * HALF_GRPS + (tile + 1))
                if tile == 0:
                    pe.wait_ge(early_feat, c + 2)
                    pe.wait_ge(repeats_feat, c + 1)
                for n in range(PER_TILE):
                    s = tile * QS + n * Q
                    half, m = divmod(n, PER_TILE // 2)
                    last = nc.tensor.matmul(
                        ps_gram[tile % 2][:, half, m * P:(m + 1) * P],
                        feat_t[:, s:s + Q, :].rearrange("d s f -> d (s f)"),
                        feat_t[:, s:s + Q, :].rearrange("d s f -> d (s f)"), start=True, stop=True)
                last.then_inc(gram_done, 1)

            def hidden1_dense(c):
                for h in range(NC1):
                    nc.tensor.matmul(ps_l1[h // 2][:, h % 2, 0:P], w1_dense[:, h * P:(h + 1) * P],
                                     early[:, 0, bass.ts(c, P)], start=(h % 2 == 0), stop=False,
                                     skip_group_check=True)

            def hidden1_pairs(c):
                pe.wait_ge(pairs_dve, (c + 1) * TILES)
                pe.wait_ge(pairs_act, (c + 1) * TILES)
                for h in range(NC1):
                    for k in range(CHUNKS):
                        last = nc.tensor.matmul(ps_l1[h // 2][:, h % 2, 0:P], w1_pairs[:, k, h * P:(h + 1) * P],
                                                pairs[:, k, :], start=False, stop=(k == CHUNKS - 1),
                                                skip_group_check=True)
                    if h % 2 == 1:
                        last.then_inc(l1_done, 1)

            def hidden2(c):
                pe.wait_ge(hid1_act, c + 1)
                for h in range(NC1):
                    if h == 2:
                        pe.wait_ge(hid1_dve, c + 1)
                    last = nc.tensor.matmul(ps_l2, hid1_t[:, h, :], w2[:, h, :], start=(h == 0), stop=(h == NC1 - 1))
                last.then_inc(l2_done, 1)

            def last_hidden2_bias():
                nc.tensor.matmul(ps_l2_last, ones[0:1, 0:P], b2[0:1, :], start=True, stop=False)

            def last_hidden2():
                pe.wait_ge(hid1_act, BLOCKS)
                for h in range(NC1):
                    if h == 2:
                        pe.wait_ge(hid1_dve, BLOCKS)
                    last = nc.tensor.matmul(ps_l2_last, hid1_t[:, h, :], w2[:, h, :], start=False, stop=(h == NC1 - 1))
                last.then_inc(l2_done, 1)

            pe.wait_ge(ones_set, 1)
            for _ in range(WARM_UP):
                nc.tensor.matmul(ps_tr[1][:, 0:2, :], ones[:, 0:P], ones[:], start=True, stop=True)
            for i in range(SEL):
                if i == SEL - 1:
                    pe.wait_ge(ident_in, 16)
                    quarter_transposes(0, 0)
                if i == 0:
                    pe.wait_ge(first_half_hi, 1)
                else:
                    pe.wait_ge(hi_done, i + 1)
                if sel_bank[i] in sel_bank[:i]:
                    pe.wait_ge(sel_done, i - sel_bank[:i][::-1].index(sel_bank[i]))
                for k in range(KSEL):
                    if i == 0 and k == HALF:
                        pe.wait_ge(hi_done, 1)
                    if k < K_DVE[i]:
                        pe.wait_ge(onehot_dve, sum(K_DVE[:i]) + k + 1)
                    else:
                        pe.wait_ge(onehot_act, i + 1)
                    nc.tensor.matmul(ps_sel[i], tbl_hi[i % 2][:, k, :], onehot[i % 2][:, k, :],
                                     start=(k == 0), stop=False)
                pe.wait_ge(lo_done, i + 1)
                for k in range(KSEL):
                    last = nc.tensor.matmul(ps_sel[i], tbl_lo[i % 2][:, k, :], onehot[i % 2][:, k, :],
                                            start=False, stop=(k == KSEL - 1))
                last.then_inc(early_psum, 1)
            quarter_transposes(0, 1)
            gram(0, 0)
            pe.wait_ge(sel_done, SEL)
            pe.wait_ge(dense_in, 16)
            pe.wait_ge(w1_dense_sum, 1)
            pe.wait_ge(w1_in, 16)
            pe.wait_ge(w2_in, 16)
            pe.wait_ge(w3_in, 32)

            def second_half(c):
                quarter_transposes(c, 2)
                gram(c, 1)
                quarter_transposes(c, 3)
                gram(c, 2)
                gram(c, 3)
                hidden1_dense(c)
                quarter_transposes(c + 1, 0)

            def hidden1_and_next_tile(c):
                hidden1_pairs(c)
                quarter_transposes(c + 1, 1)

            def hidden2_of_previous(c):
                pe.wait_ge(pairs_dve, c * TILES + 3)
                pe.wait_ge(pairs_act, c * TILES + 3)
                hidden2(c - 1)

            second_half(0)
            hidden1_and_next_tile(0)
            gram(1, 0)
            with pe.Fori(1, LAST) as c:
                second_half(c)
                hidden2_of_previous(c)
                hidden1_and_next_tile(c)
                pe.wait_ge(hid2_biased, c)
                gram(c + 1, 0)
            quarter_transposes(LAST, 2)
            gram(LAST, 1)
            gram(LAST, 2)
            quarter_transposes(LAST, 3)
            hidden1_dense(LAST)
            gram(LAST, 3)
            last_hidden2_bias()
            hidden2_of_previous(LAST)
            hidden1_pairs(LAST)
            last_hidden2()

        @block.scalar
        def _(act):
            def repeated_slots(c):
                nc.scalar.copy(feat_t[:, :, SLOTS:PAD].rearrange("d s f -> d f s"),
                               early[:, 0:REPEATED, bass.ts(c, P)]).then_inc(repeats_feat, 1)

            def early_slots(c, slots):
                nc.scalar.copy(feat_t[:, :, 0:slots].rearrange("d s f -> d f s"),
                               early[:, 0:slots, bass.ts(c, P)]).then_inc(early_feat, 1)

            def gathered_slots(c, quarter):
                i = 2 * quarter
                act.wait_ge(tr_done, c * NGRP + (i + 1))
                feat_out(nc.scalar.copy, i).then_inc(feat_act, 1)

            def pair_tails(c, tile):
                act.wait_ge(gram_done, c * TILES + (tile + 1))
                tails_out(nc.scalar.copy, tile, (0, 1)).then_inc(tails_act, 1)

            def pair_heads(c, tile):
                act.wait_ge(tails_act, c * TILES + (tile + 1))
                heads_out(nc.scalar.copy, tile, (0, 1)).then_inc(pairs_act, 1)

            def interactions(c, tile, rows_quarter=None):
                pair_tails(c, tile)
                if rows_quarter is not None:
                    gathered_slots(c, rows_quarter)
                pair_heads(c, tile)

            def later_tiles(c):
                interactions(c, 1, rows_quarter=3)
                interactions(c, 2)
                interactions(c, 3)

            def last_later_tiles():
                interactions(LAST, 1)
                interactions(LAST, 2, rows_quarter=3)
                interactions(LAST, 3)

            def hidden1(c):
                act.wait_ge(l1_done, c * 2 + 1)
                for h in range(2):
                    last = nc.scalar.activation(hid1_t[:, h, :], ps_l1[0][:, h, 0:P], ACT.Relu, bias=b1[:, h:h + 1])
                last.then_inc(hid1_act, 1)

            for i in range(SEL):
                if i == 0:
                    act.wait_ge(first_half_in, 16)
                    nc.scalar.copy(tbl_hi[i][:, 0:HALF], sel_tbl[i][:, 0:HALF]).then_inc(first_half_hi, 1)
                    act.wait_ge(sel_tbl_in[i], 16)
                    nc.scalar.copy(tbl_hi[i][:, HALF:KSEL], sel_tbl[i][:, HALF:KSEL]).then_inc(hi_done, 1)
                else:
                    act.wait_ge(sel_tbl_in[i], 16)
                    if i >= 2:
                        act.wait_ge(early_psum, i - 1)
                    nc.scalar.copy(tbl_hi[i % 2][:], sel_tbl[i][:]).then_inc(hi_done, 1)
                act.wait_ge(row_id_set, 1)
                act.wait_ge(sel_ids_in[i], 16)
                if i >= 1:
                    act.wait_ge(onehot_act, i)
                chunks = KSEL - K_DVE[i]
                for n in range(chunks):
                    k = K_DVE[i] + n
                    last = nc.scalar.activation(distance[:, n, :], sel_ids[:, i, :], ACT.Abs,
                                                bias=row_id[:, k:k + 1], scale=-1.0)
                last.then_inc(distance_done, 1)
                act.wait_ge(distance_done, i + 1)
                nc.scalar.activation(onehot[i % 2][:, K_DVE[i]:KSEL, :], distance[:, 0:chunks, :], ACT.Relu, bias=1.0,
                                     scale=-1.0).then_inc(onehot_act, 1)
                if i >= 1:
                    act.wait_ge(early_psum, i)
                    nc.scalar.copy(early[:, i, :], ps_sel[i - 1]).then_inc(sel_done, 1)
            gathered_slots(0, 0)
            act.wait_ge(dense_in, 16)
            act.wait_ge(sel_done, SEL - 1)
            repeated_slots(0)
            early_slots(0, SEL)
            act.wait_ge(early_psum, SEL)
            nc.scalar.copy(feat_t[:, :, SEL], ps_sel[SEL - 1][:, 0:P]).then_inc(early_feat, 1)
            nc.scalar.copy(early[:, SEL, :], ps_sel[SEL - 1]).then_inc(sel_done, 1)
            act.wait_ge(sel_done, SEL)
            act.wait_ge(b1_in, 16)
            gathered_slots(0, 1)
            interactions(0, 0, rows_quarter=2)
            with act.Fori(0, LAST) as c:
                later_tiles(c)
                repeated_slots(c + 1)
                early_slots(c + 1, EARLY)
                gathered_slots(c + 1, 0)
                hidden1(c)
                gathered_slots(c + 1, 1)
                interactions(c + 1, 0, rows_quarter=2)
            last_later_tiles()
            hidden1(LAST)

        @block.vector
        def _(dve):
            def gathered_slots(c, quarter):
                i = 2 * quarter + 1
                dve.wait_ge(tr_done, c * NGRP + (i + 1))
                feat_out(nc.vector.tensor_copy, i).then_inc(feat_dve, 1)

            nc.vector.memset(ones[:], 1.0).then_inc(ones_set, 1)
            dve.wait_ge(numbers_in, 16)
            nc.vector.tensor_copy(row_id[:], row_number).then_inc(row_id_set, 1)
            dve.wait_ge(row_id_set, 1)
            for i in range(SEL):
                dve.wait_ge(sel_ids_in[i], 16)
                if i >= 2:
                    dve.wait_ge(early_psum, i - 1)
                for k in range(K_DVE[i]):
                    nc.vector.tensor_scalar(onehot[i % 2][:, k, :], sel_ids[:, i, :], row_id[:, k:k + 1],
                                            None, ALU.is_equal).then_inc(onehot_dve, 1)
                dve.wait_ge(hi_done, i + 1)
                nc.vector.tensor_tensor(tbl_lo[i % 2][:], sel_tbl[i][:], tbl_hi[i % 2][:].bitcast(F32),
                                        ALU.subtract).then_inc(lo_done, 1)

            def pair_tails(c, tile):
                dve.wait_ge(gram_done, c * TILES + (tile + 1))
                tails_out(nc.vector.tensor_copy, tile, (2, 3)).then_inc(tails_dve, 1)

            def pair_heads(c, tile):
                dve.wait_ge(tails_dve, c * TILES + (tile + 1))
                heads_out(nc.vector.tensor_copy, tile, (2, 3)).then_inc(pairs_dve, 1)

            def interactions(c, tile, rows_quarter=None):
                pair_tails(c, tile)
                if rows_quarter is not None:
                    gathered_slots(c, rows_quarter)
                pair_heads(c, tile)

            def later_tiles(c):
                interactions(c, 1, rows_quarter=3)
                interactions(c, 2)
                interactions(c, 3)

            def last_later_tiles():
                interactions(LAST, 1)
                interactions(LAST, 2, rows_quarter=3)
                interactions(LAST, 3)

            def hidden1(c):
                dve.wait_ge(l1_done, c * 2 + 2)
                for h in range(2, 4):
                    last = nc.vector.tensor_scalar(hid1_t[:, h, :], ps_l1[1][:, h % 2, 0:P], b1[:, h:h + 1], 0.0,
                                                   ALU.add, ALU.max)
                last.then_inc(hid1_dve, 1)

            def output(c):
                dve.wait_ge(l2_done, c + 1)
                nc.vector.tensor_tensor(hid2[:], ps_l2, b2[:], ALU.add).then_inc(hid2_biased, 1)
                dve.wait_ge(hid2_biased, c + 1)
                nc.vector.scalar_tensor_tensor(out=hid2_w3[:], in0=hid2[:], scalar=0.0, in1=w3[:], op0=ALU.max,
                                               op1=ALU.mult, accum_out=y[:, bass.ts(c, 1)]).then_inc(y_done, 1)

            gathered_slots(0, 0)
            gathered_slots(0, 1)
            dve.wait_ge(w1_dense_in, 16)
            nc.vector.tensor_tensor(w1_dense[:], w1_dense2[:, 0, :], w1_dense2[:, 1, :],
                                    ALU.add).then_inc(w1_dense_sum, 1)
            dve.wait_ge(b1_in, 16)
            dve.wait_ge(w3_in, 32)
            interactions(0, 0, rows_quarter=2)

            def next_tile(c):
                gathered_slots(c + 1, 1)
                interactions(c + 1, 0, rows_quarter=2)

            later_tiles(0)
            gathered_slots(1, 0)
            hidden1(0)
            next_tile(0)
            with dve.Fori(1, LAST) as c:
                later_tiles(c)
                gathered_slots(c + 1, 0)
                output(c - 1)
                hidden1(c)
                next_tile(c)
            last_later_tiles()
            output(LAST - 1)
            hidden1(LAST)
            dve.wait_ge(l2_done, BLOCKS)
            nc.vector.scalar_tensor_tensor(out=hid2_w3[:].rearrange("s (a b) -> s a b", a=2), in0=ps_l2_last,
                                           scalar=0.0, in1=w3[:].rearrange("s (a b) -> s a b", a=2), op0=ALU.max,
                                           op1=ALU.mult, accum_out=y[:, LAST:BLOCKS]).then_inc(y_done, 1)


def kernel(**inputs):
    import numpy as np
    import concourse.bacc as bacc
    from concourse.bass_utils import run_bass_kernel_spmd

    nc = bacc.Bacc("TRN2", target_bir_lowering=False, num_devices=1)
    arrays = {}

    def give(name, a):
        name = "in_" + name
        arrays[name] = np.ascontiguousarray(a)
        return nc.dram_tensor(name, arrays[name].shape, mybir.dt.from_np(arrays[name].dtype),
                              kind="ExternalInput").ap()

    ids = np.asarray(inputs["ids"])
    dense = np.asarray(inputs["r_dense_features"])
    w1 = np.asarray(inputs["W_top1"])
    slot_feature = [0] + [1 + t for t in SELECTED] + [1 + t for t in GATHERED]
    tri_i, tri_j = np.triu_indices(SLOTS, k=1)
    pair_row = {(int(i), int(j)): D + n for n, (i, j) in enumerate(zip(tri_i, tri_j))}
    w1_pairs = np.zeros((P, CHUNKS, HID1), w1.dtype)
    for (f, g), (row, chunk) in pair_places().items():
        i, j = sorted((slot_feature[f], slot_feature[g]))
        w1_pairs[row, chunk] = w1[pair_row[i, j]]
    sel_tbl = np.zeros((SEL, SEL_ROWS, D), np.float32)
    for n, t in enumerate(SELECTED):
        sel_tbl[n, :inputs[f"tbl_{t}"].shape[0]] = np.asarray(inputs[f"tbl_{t}"])

    tbl_rows = [inputs[f"tbl_{t}"].shape[0] for t in GATHERED]
    first_row = np.concatenate([[0], np.cumsum(tbl_rows)[:-1]]).astype(np.int32)
    ids_cols, base_cols = [], []
    for c in range(BLOCKS):
        for gathers in PLAN:
            for t0, n, s0, ns in gathers:
                samples = slice(c * P + s0, c * P + s0 + ns)
                ids_cols.append(np.concatenate([ids[samples, GATHERED[t]] for t in range(t0, t0 + n)]))
                base_cols.append(np.repeat(first_row[t0:t0 + n], ns))

    row_number = np.arange(SEL_ROWS, dtype=np.int32).reshape(P, KSEL)
    args = [
        give("numbers", np.concatenate([np.stack(ids_cols, axis=1), np.stack(base_cols, axis=1), row_number], axis=1)),
        give("sel_ids", ids[:, list(SELECTED)].T),
        give("ident", np.eye(P, dtype=np.float32)),
        give("dense_t", dense.T),
        give("sel_tbl", sel_tbl.reshape(SEL, P, KSEL, D)),
        give("tables", np.concatenate([np.asarray(inputs[f"tbl_{t}"]) for t in GATHERED])),
        give("w1_pairs", w1_pairs),
        give("w1_dense", np.stack([w1[:D], w1[-D:]], axis=1)),
        give("b1", np.asarray(inputs["b_top1"]).reshape(NC1, P).T),
        give("w2", np.asarray(inputs["W_top2"]).reshape(NC1, P, HID2).transpose(1, 0, 2)),
        give("b2", np.asarray(inputs["b_top2"])),
        give("w3", np.asarray(inputs["W_top3"]).reshape(HID2)),
    ]
    y = nc.dram_tensor("out_y", (P, BLOCKS), F32, kind="ExternalOutput").ap()
    build(nc, *args, y)
    result = run_bass_kernel_spmd(nc, [arrays], core_ids=[0])
    return np.asarray(result.results[0]["out_y"]).T.reshape(BATCH, 1)
```
